# Optimizing a Trainium2 kernel written in Bass

```python
import numpy as np
import jax
import jax.numpy as jnp

def _softmax(x, axis=-1):
    return jax.nn.softmax(x, axis=axis)

def _gelu(x):
    return jax.nn.gelu(x, approximate=True)

def _silu(x):
    return jax.nn.silu(x)

def _sigmoid(x):
    return jax.nn.sigmoid(x)

def _layernorm(x, axis=-1, eps=1e-05):
    m = jnp.mean(x, axis=axis, keepdims=True)
    v = jnp.var(x, axis=axis, keepdims=True)
    return (x - m) / jnp.sqrt(v + eps)

def _scatter_add(tgt, idx, src, axis=0):
    return tgt.at[idx].add(src)

def _segment_sum(src, seg, n):
    return jax.ops.segment_sum(src, seg, n)
kernel_name = 'mk_seq_preln_d2_jaxref_r4_dcb6ec'

def setup_inputs(seed: int=0):
    np.random.seed(seed)
    _w = jnp.asarray

    def _L0_attn_setup():
        import jax, jax.numpy as jnp
        import numpy as np
        B, T, D, H = (4, 512, 256, 16)
        HEAD_DIM = D // H
        LOCAL_WINDOW = 128

        def _rotate_half(t):
            t1, t2 = jnp.split(t, 2, axis=-1)
            return jnp.concatenate([-t2, t1], axis=-1)

        def _apply_rope(q, k):
            Tq, d = (q.shape[2], q.shape[3])
            half = d // 2
            theta = 1.0 / 10000.0 ** (jnp.arange(half, dtype=jnp.float32) / half)
            pos = jnp.arange(Tq, dtype=jnp.float32)
            freqs = pos[:, None] * theta[None, :]
            freqs = jnp.concatenate([freqs, freqs], axis=-1)
            cos = jnp.cos(freqs)[None, None]
            sin = jnp.sin(freqs)[None, None]
            q = q * cos + _rotate_half(q) * sin
            k = k * cos + _rotate_half(k) * sin
            return (q, k)
        key = jax.random.key(seed)
        k1, k2, k3 = jax.random.split(key, 3)
        x = jax.random.normal(k1, (B, T, D), dtype=jnp.float32)
        Wqkv = jax.random.normal(k2, (D, 3 * D), dtype=jnp.float32) * 0.02
        Wout = jax.random.normal(k3, (D, D), dtype=jnp.float32) * 0.02
        return {'x': x, 'Wqkv': Wqkv, 'Wout': Wout}
    _L0_attn_in = _L0_attn_setup()

    def _L0_ffn_setup():
        import jax, jax.numpy as jnp
        import numpy as np
        D, H, N, K = (256, 512, 8, 2)
        B, S = (4, 512)
        key = jax.random.key(seed)
        ks = jax.random.split(key, 4)
        x = jax.random.normal(ks[0], (B, S, D), dtype=jnp.float32)
        Wr = jax.random.normal(ks[1], (N, D), dtype=jnp.float32) / np.sqrt(D)
        br = jnp.zeros((N,), jnp.float32)
        Wl1 = jax.random.normal(ks[2], (N, D, 2 * H), dtype=jnp.float32) / np.sqrt(D)
        bl1 = jnp.zeros((N, 2 * H), jnp.float32)
        Wl2 = jax.random.normal(ks[3], (N, H, D), dtype=jnp.float32) / np.sqrt(H)
        bl2 = jnp.zeros((N, D), jnp.float32)
        biases_N = jnp.zeros((N,), jnp.float32)
        return {'x': x, 'Wr': Wr, 'br': br, 'Wl1': Wl1, 'bl1': bl1, 'Wl2': Wl2, 'bl2': bl2, 'biases_N': biases_N}
    _L0_ffn_in = _L0_ffn_setup()

    def _L1_attn_setup():
        import jax, jax.numpy as jnp
        import numpy as np
        import math
        NUM_HEADS = 16
        DIM = 256
        DH = DIM // NUM_HEADS
        THETA = 10000.0
        SCALE_BASE = 512.0

        def _rotate_half(x):
            x = x.reshape(*x.shape[:-1], -1, 2)
            x1, x2 = (x[..., 0], x[..., 1])
            return jnp.stack((-x2, x1), axis=-1).reshape(*x1.shape[:-1], -1)

        def _xpos_rotate(q, k):
            s = q.shape[2]
            t = jnp.arange(s, dtype=jnp.float32)
            inv_freq = 1.0 / THETA ** (jnp.arange(0, DH, 2, dtype=jnp.float32) / DH)
            freqs = t[:, None] * inv_freq[None, :]
            freqs = jnp.repeat(freqs, 2, axis=-1)
            cos, sin = (jnp.cos(freqs), jnp.sin(freqs))
            base = (jnp.arange(0, DH, 2, dtype=jnp.float32) + 0.4 * DH) / (1.4 * DH)
            power = (t - s // 2) / SCALE_BASE
            scale = base[None, :] ** power[:, None]
            scale = jnp.concatenate((scale, scale), axis=-1)
            q = q * cos * scale + _rotate_half(q) * sin * scale
            inv_scale = 1.0 / scale
            k = k * cos * inv_scale + _rotate_half(k) * sin * inv_scale
            return (q, k)
        key = jax.random.key(seed)
        ks = jax.random.split(key, 5)
        b, s = (2, 512)
        w_scale = DIM ** (-0.5)
        return {'x': jax.random.normal(ks[0], (b, s, DIM), jnp.float32), 'Wq': jax.random.normal(ks[1], (DIM, DIM), jnp.float32) * w_scale, 'bq': jnp.zeros((DIM,), jnp.float32), 'Wk': jax.random.normal(ks[2], (DIM, DIM), jnp.float32) * w_scale, 'bk': jnp.zeros((DIM,), jnp.float32), 'Wv': jax.random.normal(ks[3], (DIM, DIM), jnp.float32) * w_scale, 'bv': jnp.zeros((DIM,), jnp.float32), 'Wo': jax.random.normal(ks[4], (DIM, DIM), jnp.float32) * w_scale, 'bo': jnp.zeros((DIM,), jnp.float32)}
    _L1_attn_in = _L1_attn_setup()

    def _L1_ffn_setup():
        import jax, jax.numpy as jnp
        import numpy as np
        EPS = 1e-05

        @jax.custom_vjp
        def ste_quantize(w):
            scale = jnp.maximum(jnp.mean(jnp.abs(w)), EPS)
            return jnp.clip(jnp.round(w / scale), -1.0, 1.0)

        def _ste_fwd(w):
            return (ste_quantize(w), None)

        def _ste_bwd(_, g):
            return (g,)
        ste_quantize.defvjp(_ste_fwd, _ste_bwd)
        key = jax.random.key(seed)
        k1, k2 = jax.random.split(key)
        x = jax.random.normal(k1, (8, 2048, 256), dtype=jnp.float32)
        weight = jax.random.normal(k2, (256, 256), dtype=jnp.float32) * 0.02
        return {'x': x, 'weight': weight}
    _L1_ffn_in = _L1_ffn_setup()
    _d = {'L0_attn_x': _L0_attn_in['x'], 'L0_attn_Wqkv': _L0_attn_in['Wqkv'], 'L0_attn_Wout': _L0_attn_in['Wout'], 'L0_ffn_Wr': _L0_ffn_in['Wr'], 'L0_ffn_br': _L0_ffn_in['br'], 'L0_ffn_Wl1': _L0_ffn_in['Wl1'], 'L0_ffn_bl1': _L0_ffn_in['bl1'], 'L0_ffn_Wl2': _L0_ffn_in['Wl2'], 'L0_ffn_bl2': _L0_ffn_in['bl2'], 'L0_ffn_biases_N': _L0_ffn_in['biases_N'], 'L1_attn_Wq': _L1_attn_in['Wq'], 'L1_attn_bq': _L1_attn_in['bq'], 'L1_attn_Wk': _L1_attn_in['Wk'], 'L1_attn_bk': _L1_attn_in['bk'], 'L1_attn_Wv': _L1_attn_in['Wv'], 'L1_attn_bv': _L1_attn_in['bv'], 'L1_attn_Wo': _L1_attn_in['Wo'], 'L1_attn_bo': _L1_attn_in['bo'], 'L1_ffn_weight': _L1_ffn_in['weight']}
    _x0 = _d['L0_attn_x']
    _d['L0_attn_x'] = jax.random.normal(jax.random.fold_in(jax.random.key(seed), 1), (16, 512, 256), dtype=_x0.dtype)
    del _x0
    return _d

def reference(L0_attn_x, L0_attn_Wqkv, L0_attn_Wout, L0_ffn_Wr, L0_ffn_br, L0_ffn_Wl1, L0_ffn_bl1, L0_ffn_Wl2, L0_ffn_bl2, L0_ffn_biases_N, L1_attn_Wq, L1_attn_bq, L1_attn_Wk, L1_attn_bk, L1_attn_Wv, L1_attn_bv, L1_attn_Wo, L1_attn_bo, L1_ffn_weight):

    def _L0_attn_ref(x, Wqkv, Wout):
        import jax, jax.numpy as jnp
        import numpy as np
        B, T, D, H = (4, 512, 256, 16)
        HEAD_DIM = D // H
        LOCAL_WINDOW = 128

        def _rotate_half(t):
            t1, t2 = jnp.split(t, 2, axis=-1)
            return jnp.concatenate([-t2, t1], axis=-1)

        def _apply_rope(q, k):
            Tq, d = (q.shape[2], q.shape[3])
            half = d // 2
            theta = 1.0 / 10000.0 ** (jnp.arange(half, dtype=jnp.float32) / half)
            pos = jnp.arange(Tq, dtype=jnp.float32)
            freqs = pos[:, None] * theta[None, :]
            freqs = jnp.concatenate([freqs, freqs], axis=-1)
            cos = jnp.cos(freqs)[None, None]
            sin = jnp.sin(freqs)[None, None]
            q = q * cos + _rotate_half(q) * sin
            k = k * cos + _rotate_half(k) * sin
            return (q, k)
        Bx, Tx, C = x.shape
        h, d, w = (H, HEAD_DIM, LOCAL_WINDOW)
        qkv = x @ Wqkv
        q, k, v = jnp.split(qkv, 3, axis=-1)
        q = q.reshape(Bx, Tx, h, d).transpose(0, 2, 1, 3)
        k = k.reshape(Bx, Tx, h, d).transpose(0, 2, 1, 3)
        v = v.reshape(Bx, Tx, h, d).transpose(0, 2, 1, 3)
        q, k = _apply_rope(q, k)
        idx = jnp.arange(Tx)
        dist = idx[None, :] - idx[:, None]
        allowed = (dist <= 0) & (dist >= -(w - 1))
        scores = jnp.einsum('bhqd,bhkd->bhqk', q, k) / jnp.sqrt(jnp.float32(d))
        scores = jnp.where(allowed[None, None], scores, -jnp.inf)
        weights = jax.nn.softmax(scores, axis=-1)
        out = jnp.einsum('bhqk,bhkd->bhqd', weights, v)
        out = out.transpose(0, 2, 1, 3).reshape(Bx, Tx, C)
        return out @ Wout

    def _L0_ffn_ref(x, Wr, br, Wl1, bl1, Wl2, bl2, biases_N):
        import jax, jax.numpy as jnp
        import numpy as np
        D, H, N, K = (256, 512, 8, 2)
        B, S = (4, 512)
        Bb, Ss, Dd = x.shape
        scores_BSN = jnp.einsum('bsd,nd->bsn', x, Wr) + br
        w_BSN = jax.nn.softmax(scores_BSN, axis=-1)
        _, idx_BSK = jax.lax.top_k(scores_BSN + biases_N[None, None, :], K)
        val_BSK = jnp.take_along_axis(w_BSN, idx_BSK, axis=-1)
        val_BSK = val_BSK / jnp.sum(val_BSK, axis=-1, keepdims=True)
        M = Bb * Ss
        x_MD = x.reshape(M, Dd)
        idx_MK = idx_BSK.reshape(M, K)
        val_MK = val_BSK.reshape(M, K)
        h_NM2H = jnp.einsum('md,ndh->nmh', x_MD, Wl1) + bl1[:, None, :]
        a_NMH, b_NMH = (h_NM2H[..., :H], h_NM2H[..., H:])
        y_NMD = jnp.einsum('nmh,nhd->nmd', jax.nn.silu(a_NMH) * b_NMH, Wl2) + bl2[:, None, :]
        ew_MN = jnp.zeros((M, N), x.dtype)
        ew_MN = ew_MN.at[jnp.arange(M)[:, None], idx_MK].set(val_MK)
        y_MD = jnp.einsum('mn,nmd->md', ew_MN, y_NMD)
        return y_MD.reshape(Bb, Ss, Dd)

    def _L1_attn_ref(x, Wq, bq, Wk, bk, Wv, bv, Wo, bo):
        import jax, jax.numpy as jnp
        import numpy as np
        import math
        NUM_HEADS = 16
        DIM = 256
        DH = DIM // NUM_HEADS
        THETA = 10000.0
        SCALE_BASE = 512.0

        def _rotate_half(x):
            x = x.reshape(*x.shape[:-1], -1, 2)
            x1, x2 = (x[..., 0], x[..., 1])
            return jnp.stack((-x2, x1), axis=-1).reshape(*x1.shape[:-1], -1)

        def _xpos_rotate(q, k):
            s = q.shape[2]
            t = jnp.arange(s, dtype=jnp.float32)
            inv_freq = 1.0 / THETA ** (jnp.arange(0, DH, 2, dtype=jnp.float32) / DH)
            freqs = t[:, None] * inv_freq[None, :]
            freqs = jnp.repeat(freqs, 2, axis=-1)
            cos, sin = (jnp.cos(freqs), jnp.sin(freqs))
            base = (jnp.arange(0, DH, 2, dtype=jnp.float32) + 0.4 * DH) / (1.4 * DH)
            power = (t - s // 2) / SCALE_BASE
            scale = base[None, :] ** power[:, None]
            scale = jnp.concatenate((scale, scale), axis=-1)
            q = q * cos * scale + _rotate_half(q) * sin * scale
            inv_scale = 1.0 / scale
            k = k * cos * inv_scale + _rotate_half(k) * sin * inv_scale
            return (q, k)
        b, s, _ = x.shape

        def split_heads(t):
            return t.reshape(b, s, NUM_HEADS, DH).transpose(0, 2, 1, 3)
        q_mat = split_heads(x @ Wq.T + bq)
        k_mat = split_heads(x @ Wv.T + bv)
        v_mat = split_heads(x @ Wk.T + bk)
        q_mat, k_mat = _xpos_rotate(q_mat, k_mat)
        scores = jnp.einsum('bhqd,bhkd->bhqk', q_mat, k_mat) / math.sqrt(DH * NUM_HEADS)
        causal = jnp.tril(jnp.ones((s, s), dtype=bool))
        scores = jnp.where(causal[None, None], scores, -jnp.inf)
        weights = jax.nn.softmax(scores, axis=-1)
        inter = jnp.einsum('bhqk,bhkd->bhqd', weights, v_mat)
        inter = inter.transpose(0, 2, 1, 3).reshape(b, s, DIM)
        return inter @ Wo.T + bo

    def _L1_ffn_ref(x, weight):
        import jax, jax.numpy as jnp
        import numpy as np
        EPS = 1e-05

        @jax.custom_vjp
        def ste_quantize(w):
            scale = jnp.maximum(jnp.mean(jnp.abs(w)), EPS)
            return jnp.clip(jnp.round(w / scale), -1.0, 1.0)

        def _ste_fwd(w):
            return (ste_quantize(w), None)

        def _ste_bwd(_, g):
            return (g,)
        ste_quantize.defvjp(_ste_fwd, _ste_bwd)
        w_ternary = ste_quantize(weight)
        scale = jnp.maximum(jnp.mean(jnp.abs(weight)), EPS)
        return jnp.einsum('bsi,oi->bso', x, w_ternary * scale)
    x = L0_attn_x
    x = x + _L0_attn_ref(_layernorm(x, axis=-1), L0_attn_Wqkv, L0_attn_Wout)
    x = x + _L0_ffn_ref(_layernorm(x, axis=-1), L0_ffn_Wr, L0_ffn_br, L0_ffn_Wl1, L0_ffn_bl1, L0_ffn_Wl2, L0_ffn_bl2, L0_ffn_biases_N)
    x = x + _L1_attn_ref(_layernorm(x, axis=-1), L1_attn_Wq, L1_attn_bq, L1_attn_Wk, L1_attn_bk, L1_attn_Wv, L1_attn_bv, L1_attn_Wo, L1_attn_bo)
    x = x + _L1_ffn_ref(_layernorm(x, axis=-1), L1_ffn_weight)
    return x

_drawn_inputs = setup_inputs


def setup_inputs(seed=0):
    import zlib

    import numpy as np

    out = dict(_drawn_inputs(seed))
    spreads = {'L0_ffn_br': (0.0, 0.1),
     'L0_ffn_bl1': (0.0, 0.1),
     'L0_ffn_bl2': (0.0, 0.1),
     'L0_ffn_biases_N': (0.0, 0.1),
     'L1_attn_bq': (0.0, 2.0),
     'L1_attn_bk': (0.0, 0.1),
     'L1_attn_bv': (0.0, 2.0),
     'L1_attn_bo': (0.0, 0.1)}
    factors = {}
    for name, (base, spread) in spreads.items():
        noise = np.random.default_rng([zlib.crc32(name.encode()), seed]).standard_normal(out[name].shape)
        drawn = base * np.exp(spread * noise) if base else spread * noise
        out[name] = jnp.asarray(drawn.astype(out[name].dtype))
    for name, factor in factors.items():
        out[name] = (out[name] * factor).astype(out[name].dtype)
    return out
```

```python
import numpy as np
import concourse.bass as bass
from concourse import mybir
from contextlib import ExitStack

F32 = mybir.dt.float32
F32R = mybir.dt.float32r
BF16 = mybir.dt.bfloat16
I32 = mybir.dt.int32
ALU = mybir.AluOpType
ACT = mybir.ActivationFunctionType
AX = mybir.AxisListType

B, T, D = 16, 512, 256
P = 128
NT = T // P
KC = D // P
H, DH = 16, 16
HG = 4
NG = H // HG
NE, FF = 8, 512
EPS = 1e-5
WINDOW = 128
MASKED = -1e30
Q_PART = [0, 0, 1, 1, 0, 2]
K_PART = [0, 1, 0, 1, 2, 0]
NR = len(Q_PART)
ROWS = NR * DH
AUG = ROWS + 2


class Seq:

    def __init__(self, pair, c):
        self.pair, self.c = pair, c

    def __add__(self, n):
        return Seq(self.pair, self.c + n)

    @property
    def slot(self):
        return self.c % 2

    def index(self):
        return self.c if self.pair is None else self.pair * 2 + self.c

    def count(self, per_seq, n=0):
        rest = self.c * per_seq + n
        return max(rest, 0) if self.pair is None else self.pair * (2 * per_seq) + rest

    def slot_count(self, per_use):
        rest = (self.c // 2 + 1) * per_use
        return max(rest, 0) if self.pair is None else self.pair * per_use + rest


def fresh(engine):
    engine.get_value_cache().nocache = True


def bank_steps(first, width):
    out = []
    for b in range(NT):
        w = width(b)
        per = 512 // w
        out += [(b, h, per, first(b), w) for h in range(0, HG, per)]
    return out


def attention(nc, name, x_in, x_out, w_all, w_out, tables, biases, window, scale, consts):
    ident_d, identb_d, masks_d = consts
    if window:
        s_steps = bank_steps(lambda b: max(0, b - 1) * P, lambda b: min(2, b + 1) * P)
        t_steps = bank_steps(lambda b: b * P, lambda b: min(2, NT - b) * P)
    else:
        s_steps = bank_steps(lambda b: 0, lambda b: (b + 1) * P)
        t_steps = bank_steps(lambda b: b * P, lambda b: (NT - b) * P)
    NS = len(s_steps) * NG
    p_width = [w for b, h, per, q0, w in t_steps if h == 0]
    NTAB = tables.shape[0]

    parts_d = nc.dram_tensor(f"{name}_parts_dram", [2, 2, 3, P * 2, T], BF16, kind="Internal").ap()
    nmax_d = nc.dram_tensor(f"{name}_nmax_dram", [2, 2 * H, T], BF16, kind="Internal").ap()

    ctx = ExitStack()
    with ctx:
        def sb(n, shape, dt=F32):
            return ctx.enter_context(nc.sbuf_tensor(f"{name}_{n}", shape, dt))

        semaphores = []

        def give_back():
            nc.clear_and_free_semaphores(semaphores)
            nc.all_engine_barrier()

        ctx.callback(give_back)

        def sem(n):
            semaphores.append(nc.alloc_semaphore(name=f"{name}_{n}"))
            return semaphores[-1]

        bank = [ctx.enter_context(nc.psum_tensor(f"{name}_bank{i}", [P, 512], F32)) for i in range(8)]
        WB, SB_, TB_, PVB, TRB = bank[0:2], bank[2:4], bank[4:6], bank[6], bank[7]

        wh = sb("wh", [P, KC, 3 * D], F32R)
        wl = sb("wl", [P, KC, 3 * D], F32R)
        wo = sb("wo", [P, NG, D])
        tab = sb("tab", [P, NTAB, T])
        ident = sb("ident", [P, P])
        identb = sb("identb", [P, P], BF16)
        mask = sb("mask", [P, 4, 512], BF16)
        if biases:
            bqk = sb("bqk", [P, 4])
            bvb = sb("bvb", [P, D])
            bob = sb("bob", [P, D])
        power = sb("power", [P, NT])
        xt = sb("xt", [P, NT, D])
        xn = sb("xn", [P, NT, D])
        stats = sb("stats", [P, NT, 6])
        mv = sb("mv", [P, NT, 2])
        ve = sb("ve", [P, NT])
        rstd = sb("rstd", [P, NT])
        xh = sb("xh", [P, KC, T], F32R)
        xl = sb("xl", [P, KC, T], F32R)
        rt = sb("rt", [P, 4, T])
        qk = sb("qk", [P, 2, 2, T])
        parts = sb("parts", [P, 2, 3, 2, T], BF16)
        qst = [sb(f"qst{i}", [AUG, H, T], BF16) for i in range(2)]
        kst = [sb(f"kst{i}", [AUG, H, T], BF16) for i in range(2)]
        va = [sb(f"va{i}", [P, NT, H, 32]) for i in range(2)]
        nmax = sb("nmax", [P, NT, H])
        nparts = sb("nparts", [P, NT, 2, H], BF16)
        nmt = sb("nmt", [2 * H, T], BF16)
        pr = [sb(f"pr{b}", [P, HG, p_width[b]]) for b in range(NT)]
        ou = [sb(f"ou{i}", [P, T]) for i in range(2)]
        rec = sb("rec", [P, T])
        ot = sb("ot", [P, NG, T])
        xr = sb("xr", [P, NT, D])

        carrier = sem("carrier")
        const_loaded, w_loaded, wh_done, wl_done, fills = (
            sem(n) for n in ("const_loaded", "w_loaded", "wh_done", "wl_done", "fills"))
        w_raw = rt[:, :, :].rearrange("p n t -> p (n t)")[:, 0:KC * 3 * D].rearrange("p (c n) -> p c n", c=KC)
        loads = [(tab[:, :, :], tables.rearrange("n p t -> p n t")), (wo[:, :, :], w_out),
                 (ident[:, :], ident_d), (identb[:, :], identb_d), (mask[:, :, :], masks_d)]
        if biases:
            bq2, bv2, bo2 = biases
            loads += [(bqk[:, :], bq2), (bvb[:, :], bv2.partition_broadcast(P)),
                      (bob[:, :], bo2.partition_broadcast(P))]
        with nc.Block() as block:
            @block.sync
            def _(sp):
                sp.dma_start(w_raw, w_all).then_inc(w_loaded, 16)
                for dst, src in loads:
                    sp.dma_start(dst, src).then_inc(const_loaded, 16)
                sp.wait_ge(const_loaded, 16 * len(loads))

            @block.gpsimd
            def _(pool):
                nc.gpsimd.memset(power[:, :], -0.5)
                for i in range(2):
                    nc.gpsimd.memset(va[i][:, :, :, :], 0.0).then_inc(fills, 1)
                pool.wait_ge(fills, 2)
                for i in range(2):
                    nc.gpsimd.memset(va[i][:, :, :, DH:DH + 1], 1.0).then_inc(fills, 1)
                pool.wait_ge(fills, 4)

            @block.scalar
            def _(act):
                act.wait_ge(w_loaded, 16)
                nc.scalar.copy(wh[:, :, :], w_raw).then_inc(wh_done, 1)

            @block.vector
            def _(dve):
                for i in range(2):
                    nc.vector.memset(kst[i][ROWS:AUG, :, :], 1.0)
                dve.wait_ge(wh_done, 1)
                nc.vector.tensor_tensor(wl[:, :, :], w_raw, wh[:, :, :].bitcast(F32), ALU.subtract)\
                    .then_inc(wl_done, 1)
                dve.wait_ge(wl_done, 1)

        x_loaded = sem("x_loaded")
        xres_loaded = sem("xres_loaded")
        parts_stored = sem("parts_stored")
        stack_loaded = [sem(f"stack_loaded{i}") for i in range(2)]
        nmax_stored = sem("nmax_stored")
        nmax_loaded = [sem(f"nmax_loaded{i}") for i in range(2)]
        y_stored = sem("y_stored")
        var_done = sem("var_done")
        rstd_done = sem("rstd_done")
        xn_done = sem("xn_done")
        xt_transposed = sem("xt_transposed")
        xh_done = sem("xh_done")
        xl_done = sem("xl_done")
        qk_projected = sem("qk_projected")
        qk_rotated = sem("qk_rotated")
        part0_done = sem("part0_done")
        rest1_done = sem("rest1_done")
        part1_done = sem("part1_done")
        part2_done = sem("part2_done")
        v_projected = sem("v_projected")
        v_copied = sem("v_copied")
        s_done = sem("s_done")
        max_done = sem("max_done")
        nparts_done = sem("nparts_done")
        nmt_transposed = sem("nmt_transposed")
        nmt_copied = sem("nmt_copied")
        t_done = sem("t_done")
        exp_done = sem("exp_done")
        pv_done = sem("pv_done")
        o_done = sem("o_done")
        out_projected = sem("out_projected")
        y_done = sem("y_done")
        res_done = sem("res_done")
        stats_done = sem("stats_done")
        ve_done = sem("ve_done")
        qk_read = sem("qk_read")
        nhigh_done = sem("nhigh_done")
        pv_copied = sem("pv_copied")
        sums_spread = sem("sums_spread")
        rec_done = sem("rec_done")

        def attend_order():
            units = [(g, b) for g in range(NG) for b in range(NT)]
            order = [("scores", *units[0])]
            for n, u in enumerate(units):
                if n + 1 < len(units):
                    order.append(("scores", *units[n + 1]))
                order.append(("values", *u))
            return order

        def schedule(attends, maxima, projects, outs):
            main = attend_order() if attends else []
            after = {}

            def put(n, *items):
                after.setdefault(min(n, len(main) - 1), []).extend(items)

            put(-1, ("load",))
            if outs:
                put(AT[0], ("out",))
            put(AT[0], ("residual",))
            if projects:
                for n, item in zip(AT[1:], (("stats",), ("norm",), ("turn", 0), ("turn", 1), ("project", 0),
                                            ("split", 0, 0), ("project", 1), ("split", 1, 0), ("split", 0, 1),
                                            ("split", 1, 1), ("store",))):
                    put(n, item)
            if maxima:
                units = [("maxima", g, n) for g in range(NG) for n in range(len(s_steps))]
                first, last = MAXIMA
                for k, u in enumerate(units):
                    put(first + k * (last - first) // len(units), u)
                put(last, ("minus",))
            if projects:
                put(len(main) - 1, ("stack",), ("project", "v"))
            for n, item in enumerate(main):
                if item[0] == "values" and item[2] == NT - 1:
                    after.setdefault(min(n + 2, len(main) - 1), []).insert(0, ("normalise", item[1]))
            out = after.get(-1, [])
            for n, item in enumerate(main):
                out = out + [item] + after.get(n, [])
            return out

        AT = (0, 1, 3, 5, 7, 10, 12, 14, 15, 17, 19, 20)
        MAXIMA = (3, 25)
        t_at = {}
        for g in range(NG):
            for n, st in enumerate(t_steps):
                t_at.setdefault((g, st[0]), []).append((g * len(t_steps) + n, st))

        def turn(engine, i, attends=True, maxima=True, projects=True, outs=True):
            for st in schedule(attends, maxima, projects, outs):
                engine(st, i, i + 1, i + 2)

        def all_turns(fori, engine):
            turn(engine, Seq(None, -2), attends=False, maxima=False, outs=False)
            turn(engine, Seq(None, -1), attends=False, outs=False)
            turn(engine, Seq(None, 0), outs=False)
            turn(engine, Seq(None, 1))
            with fori(1, (B - 2) // 2) as pair:
                for c in range(2):
                    turn(engine, Seq(pair, c))
            turn(engine, Seq(None, B - 2), projects=False)
            turn(engine, Seq(None, B - 1), maxima=False, projects=False)
            turn(engine, Seq(None, B), attends=False, maxima=False, projects=False)

        block = ctx.enter_context(nc.Block())

        @block.sync
        def _(sp):
            def step(st, i, s, m):
                fresh(sp)
                if st == ("load",):
                    if not (isinstance(m.index(), int) and m.index() >= B):
                        sp.wait_ge(xn_done, m.count(1))
                        sp.sem_inc(carrier, 1)
                        sp.dma_start(xt[:, :, :], x_in[m.index()].rearrange("(t p) d -> p t d", p=P))\
                            .then_inc(x_loaded, 16)
                elif st == ("residual",):
                    if not (isinstance(i.index(), int) and not 0 <= i.index() < B):
                        sp.wait_ge(y_stored, i.count(16))
                        sp.sem_inc(carrier, 1)
                        sp.dma_start(xr[:, :, :], x_in[i.index()].rearrange("(t p) d -> p t d", p=P))\
                            .then_inc(xres_loaded, 16)
                elif st == ("store",):
                    for a in range(2):
                        sp.wait_ge(part2_done, m.count(2, a + 1))
                        sp.sem_inc(carrier, 1)
                        sp.dma_start(parts_d[m.slot, a].rearrange("r (b p) n -> p (r b) n", b=2),
                                     parts[:, a].rearrange("p r b n -> p (r b) n")).then_inc(parts_stored, 16)
                elif st == ("stack",):
                    sp.wait_ge(parts_stored, (m + 1).count(32))
                    sp.sem_inc(carrier, 1)
                    sp.wait_ge(t_done, (m + -1).count(NS))
                    sp.sem_inc(carrier, 1)
                    for r in range(NR):
                        for a, dst, part in ((0, qst, Q_PART), (1, kst, K_PART)):
                            sp.dma_start(dst[m.slot][r * DH:(r + 1) * DH, :, :],
                                         parts_d[m.slot, a, part[r]].rearrange("(d h) n -> d h n", h=H))\
                                .then_inc(stack_loaded[m.slot], 16)
                elif st == ("minus",):
                    sp.wait_ge(nmt_copied, s.count(1, 1))
                    sp.sem_inc(carrier, 1)
                    sp.dma_start(nmax_d[s.slot], nmt[:, :]).then_inc(nmax_stored, 16)
                    sp.wait_ge(nmax_stored, s.count(16, 16))
                    sp.sem_inc(carrier, 1)
                    sp.dma_start(qst[s.slot][ROWS:AUG, :, :],
                                 nmax_d[s.slot].rearrange("(r h) n -> r h n", r=2))\
                        .then_inc(nmax_loaded[s.slot], 16)
                elif st == ("out",):
                    o = i + -1
                    sp.wait_ge(y_done, o.count(2, 2))
                    sp.sem_inc(carrier, 1)
                    sp.dma_start(x_out[o.index()].rearrange("(t p) d -> p t d", p=P), xr[:, :, :])\
                        .then_inc(y_stored, 16)

            all_turns(sp.Fori, step)
            sp.wait_ge(y_stored, 16 * B)

        @block.gpsimd
        def _(pool):
            def step(st, i, s, m):
                fresh(pool)
                if st == ("stats",):
                    pool.wait_ge(var_done, m.count(1, 1))
                    pool.sem_inc(carrier, 1)
                    nc.gpsimd.tensor_scalar_add(ve[:, :], mv[:, :, 1], EPS).then_inc(ve_done, 1)
                    pool.wait_ge(ve_done, m.count(1, 1))
                    nc.gpsimd.tensor_tensor(rstd[:, :], ve[:, :], power[:, :], ALU.pow).then_inc(rstd_done, 1)
                elif st[0] == "split":
                    p, a = st[1:]
                    if p == 0:
                        pool.wait_ge(part0_done, m.count(2, a + 1))
                        nc.gpsimd.tensor_tensor(qk[:, a], qk[:, a], parts[:, a, 0], ALU.subtract)\
                            .then_inc(rest1_done, 1)
                    else:
                        pool.wait_ge(part1_done, m.count(2, a + 1))
                        pool.wait_ge(rest1_done, m.count(2, a + 1))
                        nc.gpsimd.tensor_tensor(parts[:, a, 2], qk[:, a], parts[:, a, 1], ALU.subtract)\
                            .then_inc(part2_done, 1)
                elif st == ("residual",) and biases:
                    if not (isinstance(i.index(), int) and not 0 <= i.index() < B):
                        pool.wait_ge(xres_loaded, i.count(16, 16))
                        nc.gpsimd.tensor_tensor(xr[:, :, :], xr[:, :, :],
                                                bob[:, :].unsqueeze(1).broadcast_to([P, NT, D]), ALU.add)\
                            .then_inc(res_done, 1)

            all_turns(pool.Fori, step)

        @block.scalar
        def _(act):
            def step(st, i, s, m):
                fresh(act)
                if st[0] == "turn":
                    c = st[1]
                    act.wait_ge(xt_transposed, m.count(KC, c + 1))
                    if c == 0:
                        act.wait_ge(v_projected, m.count(2))
                    nc.scalar.copy(xh[:, c, :], TRB[:, :]).then_inc(xh_done, 1)
                elif st[0] == "split":
                    p, a = st[1:]
                    if p == 0:
                        act.wait_ge(qk_rotated, m.count(2, a + 1))
                        act.wait_ge(parts_stored, m.count(32))
                        nc.scalar.copy(parts[:, a, 0], qk[:, a]).then_inc(part0_done, 1)
                    else:
                        act.wait_ge(rest1_done, m.count(2, a + 1))
                        nc.scalar.copy(parts[:, a, 1], qk[:, a]).then_inc(part1_done, 1)
                elif st == ("project", "v") and not biases:
                    for n in range(2):
                        act.wait_ge(v_projected, m.count(2, n + 1))
                        if n == 0:
                            act.wait_ge(pv_done, (m + -1).count(NG * NT))
                        nc.scalar.copy(va[m.slot][:, 2 * n:2 * n + 2, :, 0:DH],
                                       WB[n][:, :].rearrange("p (t h d) -> p t h d", t=2, h=H))\
                            .then_inc(v_copied, 1)
                elif st == ("minus",):
                    act.wait_ge(nmt_transposed, s.count(1, 1))
                    act.wait_ge(nmax_stored, s.count(16))
                    nc.scalar.copy(nmt[:, :], TRB[0:2 * H, 0:T // 2].bitcast(BF16)).then_inc(nmt_copied, 1)
                elif st[0] == "values" and st[2] == NT - 1:
                    g = st[1]
                    act.wait_ge(pv_done, i.count(NG * NT, (g + 1) * NT))
                    act.wait_ge(o_done, i.count(NG, max(0, g - 1)))
                    nc.scalar.copy(ou[g % 2][:, :], PVB[:, :]).then_inc(pv_copied, 1)
                elif st[0] == "scores":
                    g, b = st[1:]
                    if g:
                        act.wait_ge(pv_done, i.count(NG * NT, (g - 1) * NT + b + 1))
                    else:
                        act.wait_ge(pv_done, i.count(NG * NT))
                    for n, (_, h, per, q0, w) in t_at[g, b]:
                        act.wait_ge(t_done, i.count(NS, n + 1))
                        nc.scalar.activation(pr[b][:, h:h + per, :],
                                             TB_[n % 2][:, 0:per * w].rearrange("p (h w) -> p h w", h=per),
                                             ACT.Exp, scale=scale).then_inc(exp_done, 1)

            all_turns(act.Fori, step)

        @block.vector
        def _(dve):
            def step(st, i, s, m):
                fresh(dve)
                if st == ("stats",):
                    dve.wait_ge(x_loaded, m.count(16, 16))
                    for t in range(NT):
                        last = nc.vector.bn_stats(stats[:, t, :], xt[:, t, :])
                    last.then_inc(stats_done, 1)
                    dve.wait_ge(stats_done, m.count(1, 1))
                    dve.sem_inc(carrier, 1)
                    for t in range(NT):
                        last = nc.vector.bn_aggr(mv[:, t, :], stats[:, t, :])
                    last.then_inc(var_done, 1)
                elif st == ("norm",):
                    dve.wait_ge(rstd_done, m.count(1, 1))
                    dve.wait_ge(xt_transposed, m.count(KC))
                    for t in range(NT):
                        last = nc.vector.tensor_scalar(xn[:, t, :], xt[:, t, :], mv[:, t, 0:1], rstd[:, t:t + 1],
                                                       ALU.subtract, ALU.mult)
                    last.then_inc(xn_done, 1)
                elif st[0] == "turn":
                    c = st[1]
                    dve.wait_ge(xh_done, m.count(KC, c + 1))
                    nc.vector.tensor_tensor(xl[:, c, :], TRB[:, :], xh[:, c, :].bitcast(F32), ALU.subtract)\
                        .then_inc(xl_done, 1)
                elif st[0] == "project" and st[1] != "v":
                    a = st[1]
                    ca, sa, cb, sb_ = (0, 1, 0, 1) if NTAB == 2 else range(4 * a, 4 * a + 4)
                    dve.wait_ge(qk_projected, m.count(2, a + 1))
                    dve.wait_ge(part2_done, m.count(2))
                    for n, (src, tb) in enumerate(((0, ca), (1, sa), (1, cb), (0, sb_))):
                        if biases:
                            last = nc.vector.scalar_tensor_tensor(
                                rt[:, n, :], WB[src][:, :], bqk[:, 2 * a + src:2 * a + src + 1], tab[:, tb, :],
                                ALU.add, ALU.mult)
                        else:
                            last = nc.vector.tensor_tensor(rt[:, n, :], WB[src][:, :], tab[:, tb, :], ALU.mult)
                    last.then_inc(qk_read, 1)
                    dve.wait_ge(qk_read, m.count(2, a + 1))
                    nc.vector.tensor_tensor(qk[:, a, 0, :], rt[:, 0, :], rt[:, 1, :], ALU.subtract)
                    nc.vector.tensor_tensor(qk[:, a, 1, :], rt[:, 2, :], rt[:, 3, :], ALU.add)\
                        .then_inc(qk_rotated, 1)
                    dve.wait_ge(qk_rotated, m.count(2, a + 1))
                elif st == ("project", "v") and biases:
                    for n in range(2):
                        dve.wait_ge(v_projected, m.count(2, n + 1))
                        if n == 0:
                            dve.wait_ge(pv_done, (m + -1).count(NG * NT))
                        for t in range(2):
                            last = nc.vector.tensor_tensor(
                                va[m.slot][:, 2 * n + t, :, 0:DH],
                                WB[n][:, t * D:(t + 1) * D].rearrange("p (h d) -> p h d", h=H),
                                bvb[:, :].rearrange("p (h d) -> p h d", h=H), ALU.add)
                        last.then_inc(v_copied, 1)
                elif st[0] == "maxima":
                    g, n = st[1:]
                    qb, h, per, _, w = s_steps[n]
                    at = g * len(s_steps) + n
                    dve.wait_ge(s_done, s.count(NS, at + 1))
                    nc.vector.tensor_reduce(nmax[:, qb, g * HG + h:g * HG + h + per],
                                            SB_[at % 2][:, 0:per * w].rearrange("p (h w) -> p h w", h=per),
                                            AX.X, ALU.max, negate=True).then_inc(max_done, 1)
                elif st == ("minus",):
                    dve.wait_ge(max_done, (s + 1).count(NS))
                    dve.wait_ge(nmt_transposed, s.count(1))
                    nc.vector.tensor_copy(nparts[:, :, 0, :], nmax[:, :, :]).then_inc(nhigh_done, 1)
                    dve.wait_ge(nhigh_done, s.count(1, 1))
                    nc.vector.tensor_tensor(nparts[:, :, 1, :], nmax[:, :, :], nparts[:, :, 0, :], ALU.subtract)\
                        .then_inc(nparts_done, 1)
                elif st[0] == "values" and st[2] == NT - 1:
                    g = st[1]
                    dve.wait_ge(o_done, i.count(NG, g))
                    dve.wait_ge(pv_copied, i.count(NG, g + 1))
                    dve.sem_inc(carrier, 1)
                    nc.vector.stream_shuffle(rec[:, :], ou[g % 2][:, :], [DH] * 32).then_inc(sums_spread, 1)
                elif st[0] == "normalise":
                    g = st[1]
                    dve.wait_ge(sums_spread, i.count(NG, g + 1))
                    nc.vector.reciprocal(rec[:, :], rec[:, :]).then_inc(rec_done, 1)
                    dve.wait_ge(rec_done, i.count(NG, g + 1))
                    if g == 0:
                        dve.wait_ge(out_projected, i.count(2))
                    nc.vector.tensor_tensor(ot[:, g, :], ou[g % 2][:, :], rec[:, :], ALU.mult).then_inc(o_done, 1)
                elif st == ("out",):
                    o = i + -1
                    if biases:
                        dve.wait_ge(res_done, o.count(1, 1))
                    else:
                        dve.wait_ge(xres_loaded, o.count(16, 16))
                    for n in range(2):
                        dve.wait_ge(out_projected, o.count(2, n + 1))
                        nc.vector.tensor_tensor(xr[:, 2 * n:2 * n + 2, :],
                                                SB_[n][:, :].rearrange("p (t d) -> p t d", t=2),
                                                xr[:, 2 * n:2 * n + 2, :], ALU.add).then_inc(y_done, 1)

            all_turns(dve.Fori, step)

        @block.tensor
        def _(pe):
            def product(out, lhs, rhs, n):
                k = 0
                for c in range(KC):
                    for l, r in ((0, 0), (1, 0), (0, 1)):
                        last = nc.tensor.matmul(out, lhs[l](c), rhs[r](c), start=(k == 0), stop=(k == 3 * KC - 1))
                        k += 1
                return last

            def step(st, i, s, m):
                fresh(pe)
                if st[0] == "turn":
                    c = st[1]
                    pe.wait_ge(xn_done, m.count(1, 1))
                    if c == 0:
                        pe.wait_ge(nmt_copied, (m + -1).count(1))
                    pe.wait_ge(xl_done, m.count(KC, c))
                    for t in range(NT):
                        last = nc.tensor.transpose(TRB[:, t * P:(t + 1) * P], xn[:, t, c * P:(c + 1) * P],
                                                   ident[:, :])
                    last.then_inc(xt_transposed, 1)
                elif st[0] == "project" and st[1] != "v":
                    a = st[1]
                    pe.wait_ge(xh_done, (m + 1).count(KC))
                    pe.wait_ge(xl_done, (m + 1).count(KC))
                    pe.wait_ge(v_copied, m.count(2))
                    if a:
                        pe.wait_ge(qk_read, m.count(2, 1))
                    for n in range(2):
                        col = (2 * a + n) * P
                        last = product(WB[n][:, :], [lambda c: wh[:, c, col:col + P], lambda c: wl[:, c, col:col + P]],
                                       [lambda c: xh[:, c, :], lambda c: xl[:, c, :]], T)
                    last.then_inc(qk_projected, 1)
                elif st == ("project", "v"):
                    pe.wait_ge(qk_read, m.count(2, 2))
                    for n in range(2):
                        for t in range(2 * n, 2 * n + 2):
                            last = product(WB[n][:, (t % 2) * D:(t % 2 + 1) * D],
                                           [lambda c: xh[:, c, t * P:(t + 1) * P], lambda c: xl[:, c, t * P:(t + 1) * P]],
                                           [lambda c: wh[:, c, 2 * D:], lambda c: wl[:, c, 2 * D:]], D)
                        last.then_inc(v_projected, 1)
                elif st[0] == "maxima":
                    g, n = st[1:]
                    qb, h, per, k0, w = s_steps[n]
                    at = g * len(s_steps) + n
                    if at == 0:
                        pe.wait_ge(stack_loaded[s.slot], s.slot_count(16 * 2 * NR))
                        pe.wait_ge(y_done, i.count(2))
                    pe.wait_ge(max_done, s.count(NS, max(0, at - 1)))
                    out = SB_[at % 2]
                    q, k = qst[s.slot], kst[s.slot]
                    for j in range(per):
                        hh = g * HG + h + j
                        last = nc.tensor.matmul(out[:, j * w:(j + 1) * w], q[0:ROWS, hh, qb * P:(qb + 1) * P],
                                                k[0:ROWS, hh, k0:k0 + w], start=(j == 0), stop=False, skip_group_check=True)
                    if window:
                        mask_it(out[:, 0:per * w], mask[:, 0 if w > P else 1, :]).then_inc(s_done, 1)
                    else:
                        mask_it(out[:, 0:per * w].rearrange("p (h w) -> p h w", h=per)[:, :, w - P:],
                                mask[:, 1, 0:per * P].rearrange("p (h w) -> p h w", h=per)).then_inc(s_done, 1)
                elif st == ("minus",):
                    pe.wait_ge(nparts_done, s.count(1, 1))
                    if not (isinstance(s.index(), int) and s.index() == B - 1):
                        pe.wait_ge(xl_done, (s + 2).count(KC))
                    for t in range(NT):
                        last = nc.tensor.transpose(TRB[0:2 * H, t * P // 2:(t + 1) * P // 2].bitcast(BF16),
                                                   nparts[:, t].rearrange("p r h -> p (r h)"), identb[:, :])
                    last.then_inc(nmt_transposed, 1)
                elif st[0] == "scores":
                    g, b = st[1:]
                    if (g, b) == (0, 0):
                        pe.wait_ge(nmax_loaded[i.slot], i.slot_count(16))
                        pe.wait_ge(stack_loaded[i.slot], i.slot_count(16 * 2 * NR))
                    q, k = qst[i.slot], kst[i.slot]
                    for n, (_, h, per, q0, w) in t_at[g, b]:
                        pe.wait_ge(exp_done, i.count(NS, max(0, n - 1)))
                        out = TB_[n % 2]
                        for j in range(per):
                            hh = g * HG + h + j
                            nc.tensor.matmul(out[:, j * w:(j + 1) * w], k[0:AUG, hh, b * P:(b + 1) * P],
                                             q[0:AUG, hh, q0:q0 + w], start=(j == 0), stop=False, skip_group_check=True)
                        if window:
                            mask_it(out[:, 0:per * w], mask[:, 2 if w > P else 3, :]).then_inc(t_done, 1)
                        else:
                            mask_it(out[:, 0:per * w].rearrange("p (h w) -> p h w", h=per)[:, :, 0:P],
                                    mask[:, 3, 0:per * P].rearrange("p (h w) -> p h w", h=per)).then_inc(t_done, 1)
                elif st[0] == "values":
                    g, b = st[1:]
                    if b == 0:
                        pe.wait_ge(pv_copied, i.count(NG, g))
                    n, (_, _, _, q0, w) = t_at[g, b][-1]
                    pe.wait_ge(exp_done, i.count(NS, n + 1))
                    if (g, b) == (0, 0):
                        pe.wait_ge(v_copied, (i + 1).count(2))
                    for j in range(HG):
                        last = nc.tensor.matmul(PVB[32 * j:32 * (j + 1), q0:q0 + w], va[i.slot][:, b, g * HG + j, :],
                                                pr[b][:, j, :], start=(b == 0), stop=(b == NT - 1), skip_group_check=True)
                    last.then_inc(pv_done, 1)
                elif st == ("out",):
                    pe.wait_ge(o_done, i.count(NG))
                    pe.wait_ge(max_done, (i if isinstance(i.index(), int) and i.index() >= B else s).count(NS))
                    for n in range(2):
                        for t in range(2 * n, 2 * n + 2):
                            for g in range(NG):
                                last = nc.tensor.matmul(SB_[n][:, (t % 2) * D:(t % 2 + 1) * D],
                                                        ot[:, g, t * P:(t + 1) * P], wo[:, g, :],
                                                        start=(g == 0), stop=(g == NG - 1))
                        last.then_inc(out_projected, 1)

            def mask_it(out, rhs):
                return nc.tensor.matmul(out, identb[:, :], rhs, start=False, stop=True, skip_group_check=True)

            all_turns(pe.Fori, step)


TILE = T
REGION = B * T + TILE
TILES = ((2 * B * T + NE * (TILE - 1)) // TILE + 1) // 2 * 2
FC = FF // P


def turns_of_two(fori, step, count):
    step(None, Seq(None, 0))
    step(Seq(None, 0), Seq(None, 1))
    step(Seq(None, 1), Seq(None, 2))
    with fori(1, count // 2 - 1) as pair:
        for c in range(2):
            step(Seq(pair, c), Seq(pair, c + 1))
    step(Seq(None, count - 2), Seq(None, count - 1))
    step(Seq(None, count - 1), None)


def route(nc, x_in, xs, wr_d, br_d, bn_d, below_d, before_d, ident_d, choice):
    gate, place, expert, taken = choice
    ctx = ExitStack()
    with ctx:
        def sb(n, shape, dt=F32):
            return ctx.enter_context(nc.sbuf_tensor(f"r_{n}", shape, dt))

        def sem(n):
            return ctx.enter_context(nc.semaphore(f"r_{n}"))

        bank = [ctx.enter_context(nc.psum_tensor(f"r_bank{i}", [P, 512], F32)) for i in range(8)]
        SCORES, PLACES = bank[4], bank[5]
        ident = sb("ident", [P, P])
        below = sb("below", [P, NE, NE])
        before = sb("before", [P, P], BF16)
        ones = sb("ones", [P, P], BF16)
        numbers = sb("numbers", [P, NE])
        wr = sb("wr", [P, KC, NE])
        wrh = sb("wrh", [P, KC, NE], F32R)
        wrl = sb("wrl", [P, KC, NE], F32R)
        brb = sb("brb", [P, NE])
        bnb = sb("bnb", [P, NE])
        power = sb("power", [P, NT])
        xt = [sb(f"xt{i}", [P, NT, D]) for i in range(2)]
        xn = [sb(f"xn{i}", [P, NT, D]) for i in range(2)]
        stats = sb("stats", [P, NT, 6])
        mv = sb("mv", [P, NT, 2])
        ve = sb("ve", [P, NT])
        rstd = sb("rstd", [P, NT])
        xh = sb("xh", [P, KC, T], F32R)
        xl = sb("xl", [P, KC, T], F32R)
        sc = sb("sc", [P, NT, NE])
        bs = sb("bs", [P, NT, NE])
        ex = sb("ex", [P, NT, NE])
        gt = sb("gt", [P, NT, NE, NE])
        ge = sb("ge", [P, NT, NE, NE])
        rank = sb("rank", [P, NT, NE])
        red = sb("red", [P, 4, NT])
        hot = sb("hot", [P, 2, NT, NE])
        picked = sb("picked", [P, 3, 2, NT, NE])
        weight = sb("weight", [P, 2, NT])
        spot = sb("spot", [P, 2, NT])
        who = sb("who", [P, 2, NT])
        chosen = sb("chosen", [P, NT, NE], BF16)
        pos = sb("pos", [P, NT, NE])
        row = [sb(f"row{i}", [P, 2, NT], I32) for i in range(2)]

        carrier = sem("carrier")
        const_loaded, setup = sem("const_loaded"), sem("setup")
        x_loaded = [sem(f"x_loaded{i}") for i in range(2)]
        scattered = [sem(f"scattered{i}") for i in range(2)]
        stats_done, var_done, ve_done, rstd_done, xn_done = (
            sem(n) for n in ("stats_done", "var_done", "ve_done", "rstd_done", "xn_done"))
        transposed = sem("transposed")
        xh_done = sem("xh_done")
        xl_done = sem("xl_done")
        scored = sem("scored")
        shifted = sem("shifted")
        exped = sem("exped")
        chosen_done = sem("chosen_done")
        placed = sem("placed")
        rows_done = sem("rows_done")
        gates_step = sem("gates_step")
        rows_step = sem("rows_step")
        GATES, ROWS_STEPS = 14, 5

        with nc.Block() as block:
            @block.sync
            def _(sp):
                loads = ((ident[:, :], ident_d), (below[:, :, :], below_d.partition_broadcast(P)),
                         (before[:, :], before_d), (wr[:, :, :], wr_d), (brb[:, :], br_d.partition_broadcast(P)),
                         (bnb[:, :], bn_d.partition_broadcast(P)))
                for dst, src in loads:
                    sp.dma_start(dst, src).then_inc(const_loaded, 16)
                sp.wait_ge(const_loaded, 16 * len(loads))

            @block.vector
            def _(dve):
                nc.vector.memset(ones[:, :], 1.0)
                nc.vector.memset(power[:, :], -0.5)
                for e in range(NE):
                    nc.vector.memset(numbers[:, e:e + 1], float(e))
                nc.vector.memset(taken[:, :], 0.0).then_inc(setup, 1)
                dve.wait_ge(const_loaded, 16 * 6)
                nc.vector.tensor_copy(wrh[:, :, :], wr[:, :, :]).then_inc(setup, 1)
                dve.wait_ge(setup, 2)
                nc.vector.tensor_tensor(wrl[:, :, :], wr[:, :, :], wrh[:, :, :].bitcast(F32), ALU.subtract)\
                    .then_inc(setup, 1)
                dve.wait_ge(setup, 3)

        with nc.Block() as block:
            @block.sync
            def _(sp):
                def step(s, m):
                    fresh(sp)
                    if m:
                        sp.wait_ge(xn_done, (m + -1).count(1))
                        sp.sem_inc(carrier, 1)
                        sp.dma_start(xt[m.slot][:, :, :], x_in[m.index()].rearrange("(t p) d -> p t d", p=P))\
                            .then_inc(x_loaded[m.slot], 16)

                turns_of_two(sp.Fori, step, B)

            @block.gpsimd
            def _(pool):
                def step(s, m):
                    fresh(pool)
                    if m:
                        pool.wait_ge(var_done, m.count(1, 1))
                        pool.sem_inc(carrier, 1)
                        nc.gpsimd.tensor_scalar_add(ve[:, :], mv[:, :, 1], EPS).then_inc(ve_done, 1)
                        pool.wait_ge(ve_done, m.count(1, 1))
                        nc.gpsimd.tensor_tensor(rstd[:, :], ve[:, :], power[:, :], ALU.pow).then_inc(rstd_done, 1)
                    if s:
                        pool.wait_ge(rows_done, s.count(1, 1))
                        pool.sem_inc(carrier, 1)
                        for k in range(2):
                            for t in range(NT):
                                pool.indirect_dma_start(
                                    xs, bass.IndirectOffsetOnAxis(ap=row[s.slot][:, k, t:t + 1], axis=0),
                                    xn[s.slot][:, t, :], None).then_inc(scattered[s.slot], 16)

                turns_of_two(pool.Fori, step, B)
                for i in range(2):
                    pool.wait_ge(scattered[i], 16 * 2 * NT * (B // 2))

            @block.scalar
            def _(act):
                def step(s, m):
                    fresh(act)
                    if s:
                        act.wait_ge(shifted, s.count(1, 1))
                        nc.scalar.activation(ex[:, :, :], sc[:, :, :], ACT.Exp).then_inc(exped, 1)
                    if m:
                        for c in range(KC):
                            act.wait_ge(transposed, m.count(KC, c + 1))
                            if c == 0:
                                act.wait_ge(scored, m.count(1))
                            nc.scalar.copy(xh[:, c, :], bank[c][:, :]).then_inc(xh_done, 1)

                turns_of_two(act.Fori, step, B)

            @block.vector
            def _(dve):
                def by_token(v):
                    return v.unsqueeze(2).broadcast_to([P, NT, NE])

                def over(v, axis):
                    return v.unsqueeze(axis).broadcast_to([P, NT, NE, NE])

                def choices(v):
                    return v.unsqueeze(1).broadcast_to([P, 2, NT, NE])

                def step(s, m):
                    fresh(dve)
                    if m:
                        dve.wait_ge(x_loaded[m.slot], m.slot_count(16))
                        x = xt[m.slot]
                        for t in range(NT):
                            last = nc.vector.bn_stats(stats[:, t, :], x[:, t, :])
                        last.then_inc(stats_done, 1)
                        dve.wait_ge(stats_done, m.count(1, 1))
                        dve.sem_inc(carrier, 1)
                        for t in range(NT):
                            last = nc.vector.bn_aggr(mv[:, t, :], stats[:, t, :])
                        last.then_inc(var_done, 1)
                    if s:
                        done = [0]

                        def then(instruction):
                            done[0] += 1
                            instruction.then_inc(gates_step, 1)
                            dve.wait_ge(gates_step, s.count(GATES, done[0]))

                        dve.wait_ge(scored, s.count(1, 1))
                        then(nc.vector.tensor_tensor(
                            sc[:, :, :], SCORES[:, 0:NT * NE].rearrange("p (t e) -> p t e", e=NE),
                            brb[:, :].unsqueeze(1).broadcast_to([P, NT, NE]), ALU.add))
                        nc.vector.tensor_tensor(bs[:, :, :], sc[:, :, :],
                                                bnb[:, :].unsqueeze(1).broadcast_to([P, NT, NE]), ALU.add)
                        then(nc.vector.tensor_reduce(red[:, 0, :], sc[:, :, :], AX.X, ALU.max))
                        nc.vector.tensor_tensor(sc[:, :, :], sc[:, :, :], by_token(red[:, 0, :]), ALU.subtract)\
                            .then_inc(shifted, 1)
                        nc.vector.tensor_tensor(gt[:, :, :, :], over(bs[:, :, :], 2), over(bs[:, :, :], 3), ALU.is_gt)
                        then(nc.vector.tensor_tensor(ge[:, :, :, :], over(bs[:, :, :], 2), over(bs[:, :, :], 3),
                                                     ALU.is_ge))
                        then(nc.vector.tensor_tensor(ge[:, :, :, :], ge[:, :, :, :],
                                                     below[:, :, :].unsqueeze(1).broadcast_to([P, NT, NE, NE]), ALU.mult))
                        then(nc.vector.tensor_tensor(gt[:, :, :, :], ge[:, :, :, :], gt[:, :, :, :], ALU.max))
                        then(nc.vector.tensor_reduce(rank[:, :, :], gt[:, :, :, :], AX.X, ALU.add))
                        for k in range(2):
                            last = nc.vector.tensor_scalar(hot[:, k, :, :], rank[:, :, :], float(k), None, ALU.is_equal)
                        nc.vector.tensor_scalar(chosen[:, :, :], rank[:, :, :], 1.5, None, ALU.is_lt)\
                            .then_inc(chosen_done, 1)
                        dve.wait_ge(chosen_done, s.count(1, 1))
                        dve.wait_ge(exped, s.count(1, 1))
                        then(nc.vector.tensor_reduce(red[:, 1, :], ex[:, :, :], AX.X, ALU.add))
                        then(nc.vector.reciprocal(red[:, 1, :], red[:, 1, :]))
                        then(nc.vector.tensor_tensor(ex[:, :, :], ex[:, :, :], by_token(red[:, 1, :]), ALU.mult))
                        nc.vector.tensor_tensor(picked[:, 1], hot[:, :, :, :],
                                                numbers[:, :].unsqueeze(1).unsqueeze(1).broadcast_to([P, 2, NT, NE]),
                                                ALU.mult)
                        then(nc.vector.tensor_tensor(picked[:, 0], hot[:, :, :, :], choices(ex[:, :, :]), ALU.mult))
                        nc.vector.tensor_reduce(who[:, :, :], picked[:, 1], AX.X, ALU.add)
                        then(nc.vector.tensor_reduce(weight[:, :, :], picked[:, 0], AX.X, ALU.add))
                        then(nc.vector.tensor_tensor(red[:, 2, :], weight[:, 0, :], weight[:, 1, :], ALU.add))
                        then(nc.vector.reciprocal(red[:, 3, :], red[:, 2, :]))
                        at = bass.ds(s.index() * NT, NT)
                        nc.vector.tensor_copy(expert[:, :, at], who[:, :, :])
                        then(nc.vector.tensor_tensor(gate[:, :, at], weight[:, :, :],
                                                     red[:, 3, :].unsqueeze(1).broadcast_to([P, 2, NT]), ALU.mult))
                        assert done[0] == GATES, done
                    if m:
                        dve.wait_ge(rstd_done, m.count(1, 1))
                        dve.wait_ge(transposed, (m + -1).count(KC))
                        dve.wait_ge(scattered[m.slot], (m + -2).slot_count(16 * 2 * NT))
                        for t in range(NT):
                            last = nc.vector.tensor_scalar(xn[m.slot][:, t, :], x[:, t, :], mv[:, t, 0:1],
                                                           rstd[:, t:t + 1], ALU.subtract, ALU.mult)
                        last.then_inc(xn_done, 1)
                        for c in range(KC):
                            dve.wait_ge(xh_done, m.count(KC, c + 1))
                            nc.vector.tensor_tensor(xl[:, c, :], bank[c][:, :], xh[:, c, :].bitcast(F32), ALU.subtract)\
                                .then_inc(xl_done, 1)
                    if s:
                        done = [0]

                        def next_(instruction):
                            done[0] += 1
                            instruction.then_inc(rows_step, 1)
                            dve.wait_ge(rows_step, s.count(ROWS_STEPS, done[0]))

                        dve.wait_ge(placed, s.count(1, 1))
                        next_(nc.vector.tensor_tensor(
                            pos[:, :, :], PLACES[:, 0:NT * NE].rearrange("p (t e) -> p t e", e=NE),
                            taken[:, :].unsqueeze(1).broadcast_to([P, NT, NE]), ALU.add))
                        nc.vector.tensor_tensor(taken[:, :], PLACES[:, NT * NE:(NT + 1) * NE], taken[:, :], ALU.add)
                        next_(nc.vector.tensor_tensor(picked[:, 2], hot[:, :, :, :], choices(pos[:, :, :]), ALU.mult))
                        next_(nc.vector.tensor_reduce(spot[:, :, :], picked[:, 2], AX.X, ALU.add))
                        next_(nc.vector.tensor_copy(place[:, :, at], spot[:, :, :]))
                        next_(nc.vector.scalar_tensor_tensor(who[:, :, :], who[:, :, :], float(REGION), spot[:, :, :],
                                                             ALU.mult, ALU.add))
                        nc.vector.tensor_copy(row[s.slot][:, :, :], who[:, :, :]).then_inc(rows_done, 1)
                        assert done[0] == ROWS_STEPS, done

                turns_of_two(dve.Fori, step, B)

            @block.tensor
            def _(pe):
                def step(s, m):
                    fresh(pe)
                    if s:
                        pe.wait_ge(xl_done, (s + 1).count(KC))
                        for t in range(NT):
                            p = 0
                            for c in range(KC):
                                for x, w in ((xh, wrh), (xl, wrh), (xh, wrl)):
                                    last = nc.tensor.matmul(SCORES[:, t * NE:(t + 1) * NE], x[:, c, t * P:(t + 1) * P],
                                                            w[:, c, :], start=(p == 0), stop=(p == 3 * KC - 1))
                                    p += 1
                        last.then_inc(scored, 1)
                    if m:
                        pe.wait_ge(xn_done, m.count(1, 1))
                        pe.wait_ge(xl_done, m.count(KC))
                        for c in range(KC):
                            for t in range(NT):
                                last = nc.tensor.transpose(bank[c][:, t * P:(t + 1) * P],
                                                           xn[m.slot][:, t, c * P:(c + 1) * P], ident[:, :])
                            last.then_inc(transposed, 1)
                    if s:
                        pe.wait_ge(chosen_done, s.count(1, 1))
                        pe.wait_ge(rows_done, s.count(1))
                        for t in range(NT + 1):
                            out = PLACES[:, t * NE:(t + 1) * NE]
                            for b in range(t):
                                last = nc.tensor.matmul(out, ones[:, :], chosen[:, b, :], start=(b == 0),
                                                        stop=(b == NT - 1))
                            if t < NT:
                                last = nc.tensor.matmul(out, before[:, :], chosen[:, t, :], start=(t == 0), stop=True)
                        last.then_inc(placed, 1)

                turns_of_two(pe.Fori, step, B)


def experts(nc, xs, ys, w1_d, b1_d, w2_d, b2_d, starts_d, ident_d, choice, yrow):
    gate, place, expert, taken = choice
    ctx = ExitStack()
    with ctx:
        def sb(n, shape, dt=F32):
            return ctx.enter_context(nc.sbuf_tensor(f"e_{n}", shape, dt))

        def sem(n):
            return ctx.enter_context(nc.semaphore(f"e_{n}"))

        bank = [ctx.enter_context(nc.psum_tensor(f"e_bank{i}", [P, 512], F32)) for i in range(8)]
        AB, BB, YB, TB = bank[0:2], bank[2:4], bank[4:6], bank[6:8]
        NW = KC * 2 * FF + FC * D
        ident = sb("ident", [P, P])
        zeros = sb("zeros", [P, NT, D])
        tab = sb("tab", [1, 2, TILES], I32)
        rows = sb("rows", [1, NE], I32)
        w_raw = [sb(f"w_raw{i}", [P, NW]) for i in range(2)]
        wh = [sb(f"wh{i}", [P, NW], F32R) for i in range(2)]
        wl = [sb(f"wl{i}", [P, NW], F32R) for i in range(2)]
        b1 = [sb(f"b1{i}", [P, 2 * FC]) for i in range(2)]
        b2 = [sb(f"b2{i}", [P, D]) for i in range(2)]
        xg = sb("xg", [P, NT, D])
        xh = [sb(f"xh{i}", [P, KC, T], F32R) for i in range(2)]
        xl = [sb(f"xl{i}", [P, KC, T], F32R) for i in range(2)]
        sa = [sb(f"sa{i}", [P, T]) for i in range(2)]
        gf = [sb(f"gf{i}", [P, T]) for i in range(2)]
        gh = [sb(f"gh{i}", [P, FC, T], F32R) for i in range(2)]
        gl = [sb(f"gl{i}", [P, FC, T], F32R) for i in range(2)]
        yt = sb("yt", [P, NT, D])

        def first(w):
            return w[:, 0:KC * 2 * FF].rearrange("p (c n) -> p c n", c=KC)

        def second(w):
            return w[:, KC * 2 * FF:].rearrange("p (c n) -> p c n", c=FC)

        carrier = sem("carrier")
        const_loaded, plan_step, plan_done, padded = (sem(n) for n in ("const_loaded", "plan_step", "plan_done", "padded"))
        x_loaded = sem("x_loaded")
        w_loaded = [sem(f"w_loaded{i}") for i in range(2)]
        b_loaded = [sem(f"b_loaded{i}") for i in range(2)]
        y_stored = sem("y_stored")
        transposed = sem("transposed")
        xh_done = sem("xh_done")
        xl_done = sem("xl_done")
        wh_done = sem("wh_done")
        wl_done = sem("wl_done")
        ab_done = sem("ab_done")
        silu_done = sem("silu_done")
        gf_done = sem("gf_done")
        gh_done = sem("gh_done")
        gl_done = sem("gl_done")
        y_projected = sem("y_projected")
        y_done = sem("y_done")

        with ExitStack() as inner:
            def tmp(n, shape, dt=F32):
                return inner.enter_context(nc.sbuf_tensor(f"e_{n}", shape, dt))

            NJ = B * T // TILE
            starts = tmp("starts", [P, NE + NE * NE + TILES + NJ])
            numbers = starts[:, 0:NE]
            below = starts[:, NE:NE + NE * NE].rearrange("p (i j) -> p i j", j=NE)
            tile = starts[:, NE + NE * NE:NE + NE * NE + TILES]
            full = starts[:, NE + NE * NE + TILES:]
            many = tmp("many", [P, NE, NJ])
            tiles = tmp("tiles", [P, NE])
            prod = tmp("prod", [P, NE, NE])
            start = tmp("start", [P, NE])
            end = tmp("end", [P, NE])
            last_ = tmp("last", [P, 1])
            tc = tmp("tc", [P, TILES])
            past = tmp("past", [P, TILES, NE])
            who = tmp("who", [P, TILES])
            off = tmp("off", [P, NE])
            of = tmp("of", [P, TILES, NE])
            at = tmp("at", [P, TILES])
            same = tmp("same", [P, 2, B * NT, NE])
            base = tmp("base", [P, 2, B * NT])
            with nc.Block() as block:
                @block.sync
                def _(sp):
                    sp.dma_start(ident[:, :], ident_d).then_inc(const_loaded, 16)
                    sp.dma_start(starts[:, :], starts_d.partition_broadcast(P)).then_inc(const_loaded, 16)
                    sp.wait_ge(plan_done, 1)
                    for e in range(NE):
                        n = sp.value_load(rows[0:1, e:e + 1], min_val=0, max_val=B * T)
                        sp.dma_start(xs[bass.ds(n + e * REGION, TILE), :].rearrange("(t p) d -> p t d", p=P),
                                     zeros[:, :, :]).then_inc(padded, 16)
                    sp.wait_ge(padded, 16 * NE)

                @block.vector
                def _(dve):
                    done = [0]

                    def then(instruction):
                        done[0] += 1
                        instruction.then_inc(plan_step, 1)
                        dve.wait_ge(plan_step, done[0])

                    def by_expert(v, n):
                        return v.unsqueeze(2).broadcast_to([P, n, NE])

                    def experts_of(v, n):
                        return v.unsqueeze(1).broadcast_to([P, n, NE])

                    nc.vector.memset(zeros[:, :, :], 0.0)
                    dve.wait_ge(const_loaded, 32)
                    then(nc.vector.tensor_tensor(many[:, :, :], taken[:, :].unsqueeze(2).broadcast_to([P, NE, NJ]),
                                                 full.unsqueeze(1).broadcast_to([P, NE, NJ]), ALU.is_gt))
                    then(nc.vector.tensor_reduce(tiles[:, :], many[:, :, :], AX.X, ALU.add))
                    then(nc.vector.tensor_tensor(prod[:, :, :], below, experts_of(tiles[:, :], NE), ALU.mult))
                    then(nc.vector.tensor_reduce(start[:, :], prod[:, :, :], AX.X, ALU.add))
                    then(nc.vector.tensor_tensor(end[:, :], start[:, :], tiles[:, :], ALU.add))
                    then(nc.vector.tensor_scalar(last_[:, :], end[:, NE - 1:NE], -1.0, None, ALU.add))
                    then(nc.vector.tensor_scalar(tc[:, :], tile, last_[:, 0:1], None, ALU.min))
                    then(nc.vector.tensor_tensor(past[:, :, :], by_expert(tc[:, :], TILES), experts_of(end[:, :], TILES),
                                                 ALU.is_ge))
                    then(nc.vector.tensor_reduce(who[:, :], past[:, :, :], AX.X, ALU.add))
                    then(nc.vector.tensor_scalar(off[:, :], start[:, :], -float(TILE), None, ALU.mult))
                    then(nc.vector.scalar_tensor_tensor(off[:, :], numbers, float(REGION), off[:, :], ALU.mult, ALU.add))
                    then(nc.vector.tensor_tensor(of[:, :, :], experts_of(numbers, TILES), by_expert(who[:, :], TILES),
                                                 ALU.is_equal))
                    then(nc.vector.tensor_tensor(of[:, :, :], of[:, :, :], experts_of(off[:, :], TILES), ALU.mult))
                    then(nc.vector.tensor_reduce(at[:, :], of[:, :, :], AX.X, ALU.add))
                    then(nc.vector.scalar_tensor_tensor(at[:, :], tc[:, :], float(TILE), at[:, :], ALU.mult, ALU.add))
                    nc.vector.tensor_copy(tab[:, 0, :], who[0:1, :])
                    nc.vector.tensor_copy(tab[:, 1, :], at[0:1, :])
                    nc.vector.tensor_copy(rows[:, :], taken[0:1, :]).then_inc(plan_done, 1)
                    for k in range(2):
                        then(nc.vector.tensor_tensor(same[:, k], experts_of(numbers, B * NT),
                                                     by_expert(expert[:, k, :], B * NT), ALU.is_equal))
                        then(nc.vector.tensor_tensor(same[:, k], same[:, k], experts_of(start[:, :], B * NT), ALU.mult))
                        then(nc.vector.tensor_reduce(base[:, k], same[:, k], AX.X, ALU.add))
                    then(nc.vector.scalar_tensor_tensor(base[:, :, :], base[:, :, :], float(TILE), place[:, :, :],
                                                        ALU.mult, ALU.add))
                    then(nc.vector.tensor_copy(yrow[:, :, :], base[:, :, :]))
                    dve.wait_ge(plan_done, 1)

        with nc.Block() as block:
            @block.sync
            def _(sp):
                def step(s, m):
                    fresh(sp)
                    if m:
                        i = m.index()
                        e = sp.value_load(tab[0:1, 0, bass.ds(i, 1)], min_val=0, max_val=NE - 1)
                        r = sp.value_load(tab[0:1, 1, bass.ds(i, 1)], min_val=0, max_val=NE * REGION - TILE)
                        sp.wait_ge(transposed, m.count(KC))
                        sp.sem_inc(carrier, 1)
                        sp.dma_start(xg[:, :, :], xs[bass.ds(r, TILE), :].rearrange("(t p) d -> p t d", p=P))\
                            .then_inc(x_loaded, 16)
                        sp.wait_ge(wl_done, (m + -1).count(2))
                        sp.sem_inc(carrier, 1)
                        sp.dma_start(first(w_raw[m.slot]), w1_d[e]).then_inc(w_loaded[m.slot], 16)
                        sp.dma_start(second(w_raw[m.slot]), w2_d[e]).then_inc(w_loaded[m.slot], 16)
                        sp.wait_ge(y_done, (m + -1).count(2))
                        sp.sem_inc(carrier, 1)
                        sp.dma_start(b1[m.slot][:, :], b1_d[e]).then_inc(b_loaded[m.slot], 16)
                        sp.dma_start(b2[m.slot][:, :], b2_d[e].partition_broadcast(P)).then_inc(b_loaded[m.slot], 16)

                turns_of_two(sp.Fori, step, TILES)

            @block.gpsimd
            def _(pool):
                def store(s):
                    pool.wait_ge(y_done, s.count(2, 2))
                    pool.sem_inc(carrier, 1)
                    pool.dma_start(ys[bass.ds(s.index() * TILE, TILE), :].rearrange("(t p) d -> p t d", p=P),
                                   yt[:, :, :]).then_inc(y_stored, 16)

                def step(s, m):
                    fresh(pool)
                    if m:
                        for n, part in enumerate((first, second)):
                            pool.wait_ge(wh_done, m.count(2, n + 1))
                            nc.gpsimd.tensor_tensor(part(wl[m.slot]), part(w_raw[m.slot]),
                                                    part(wh[m.slot]).bitcast(F32), ALU.subtract).then_inc(wl_done, 1)
                    if s and not (isinstance(s.index(), int) and s.index() == 0):
                        store(s + -1)
                    if s and not m:
                        store(s)

                turns_of_two(pool.Fori, step, TILES)
                pool.wait_ge(y_stored, 16 * TILES)

            @block.scalar
            def _(act):
                def step(s, m):
                    fresh(act)
                    for f in range(FC):
                        if s:
                            act.wait_ge(ab_done, s.count(FC, f + 1))
                            if f == 0:
                                act.wait_ge(b_loaded[s.slot], s.slot_count(32))
                            nc.scalar.activation(sa[f % 2][:, :], AB[f % 2][:, :], ACT.Silu,
                                                 bias=b1[s.slot][:, f:f + 1]).then_inc(silu_done, 1)
                            act.wait_ge(gf_done, s.count(FC, f + 1))
                            if f == 0:
                                act.wait_ge(y_projected, (s + -1).count(2))
                            nc.scalar.copy(gh[s.slot][:, f, :], gf[f % 2][:, :]).then_inc(gh_done, 1)
                        if m and f < KC:
                            act.wait_ge(transposed, m.count(KC, f + 1))
                            nc.scalar.copy(xh[m.slot][:, f, :], TB[f][:, :]).then_inc(xh_done, 1)
                        if m and f in (0, 2):
                            part = second if f else first
                            if f == 0:
                                act.wait_ge(w_loaded[m.slot], m.slot_count(32))
                                act.wait_ge(ab_done, (m + -1).count(FC))
                            else:
                                act.wait_ge(y_projected, (m + -1).count(2))
                            nc.scalar.copy(part(wh[m.slot]), part(w_raw[m.slot])).then_inc(wh_done, 1)

                turns_of_two(act.Fori, step, TILES)

            @block.vector
            def _(dve):
                def outputs(s):
                    dve.wait_ge(y_stored, s.count(16))
                    for n in range(2):
                        dve.wait_ge(y_projected, s.count(2, n + 1))
                        nc.vector.tensor_tensor(yt[:, 2 * n:2 * n + 2, :],
                                                YB[n][:, :].rearrange("p (t d) -> p t d", t=2),
                                                b2[s.slot][:, :].unsqueeze(1).broadcast_to([P, 2, D]), ALU.add)\
                            .then_inc(y_done, 1)

                def step(s, m):
                    fresh(dve)
                    for f in range(FC):
                        if s:
                            dve.wait_ge(silu_done, s.count(FC, f + 1))
                            dve.wait_ge(b_loaded[s.slot], s.slot_count(32))
                            nc.vector.scalar_tensor_tensor(
                                gf[f % 2][:, :], BB[f % 2][:, :], b1[s.slot][:, FC + f:FC + f + 1],
                                sa[f % 2][:, :], ALU.add, ALU.mult).then_inc(gf_done, 1)
                            dve.wait_ge(gh_done, s.count(FC, f + 1))
                            nc.vector.tensor_tensor(gl[s.slot][:, f, :], gf[f % 2][:, :],
                                                    gh[s.slot][:, f, :].bitcast(F32), ALU.subtract).then_inc(gl_done, 1)
                        if m and f < KC:
                            dve.wait_ge(xh_done, m.count(KC, f + 1))
                            nc.vector.tensor_tensor(xl[m.slot][:, f, :], TB[f][:, :],
                                                    xh[m.slot][:, f, :].bitcast(F32), ALU.subtract).then_inc(xl_done, 1)
                        if s and f == 1 and not (isinstance(s.index(), int) and s.index() == 0):
                            outputs(s + -1)
                    if s and not m:
                        outputs(s)

                turns_of_two(dve.Fori, step, TILES)

            @block.tensor
            def _(pe):
                def hidden(s, f):
                    pe.wait_ge(silu_done, s.count(FC, max(0, f - 1)))
                    pe.wait_ge(gf_done, s.count(FC, max(0, f - 1)))
                    for out, col in ((AB[f % 2], f * P), (BB[f % 2], FF + f * P)):
                        p = 0
                        for kc in range(KC):
                            for w, x in ((wh, xh), (wl, xh), (wh, xl)):
                                last = nc.tensor.matmul(out[:, :], first(w[s.slot])[:, kc, col:col + P],
                                                        x[s.slot][:, kc, :], start=(p == 0), stop=(p == 3 * KC - 1))
                                p += 1
                    last.then_inc(ab_done, 1)

                def output(s):
                    pe.wait_ge(gl_done, (s + 1).count(FC))
                    pe.wait_ge(wl_done, s.count(2, 2))
                    pe.wait_ge(y_done, s.count(2))
                    for n in range(2):
                        for t in range(2 * n, 2 * n + 2):
                            p = 0
                            for f in range(FC):
                                for x, w in ((gh, wh), (gl, wh), (gh, wl)):
                                    last = nc.tensor.matmul(YB[n][:, (t % 2) * D:(t % 2 + 1) * D],
                                                            x[s.slot][:, f, t * P:(t + 1) * P],
                                                            second(w[s.slot])[:, f, :],
                                                            start=(p == 0), stop=(p == 3 * FC - 1))
                                    p += 1
                        last.then_inc(y_projected, 1)

                def step(s, m):
                    fresh(pe)
                    for f in range(FC):
                        if s:
                            if f == 0:
                                pe.wait_ge(xl_done, (s + 1).count(KC))
                                pe.wait_ge(wl_done, s.count(2, 1))
                            hidden(s, f)
                        if m and f == 0:
                            pe.wait_ge(x_loaded, m.count(16, 16))
                            pe.wait_ge(xl_done, m.count(KC))
                            for c in range(KC):
                                for t in range(NT):
                                    last = nc.tensor.transpose(TB[c][:, t * P:(t + 1) * P],
                                                               xg[:, t, c * P:(c + 1) * P], ident[:, :])
                                last.then_inc(transposed, 1)
                        if s and f == 1 and not (isinstance(s.index(), int) and s.index() == 0):
                            output(s + -1)
                    if s and not m:
                        output(s)

                turns_of_two(pe.Fori, step, TILES)


def combine(nc, x_in, x_out, ys, gate, yrow):
    ctx = ExitStack()
    with ctx:
        def sb(n, shape, dt=F32):
            return ctx.enter_context(nc.sbuf_tensor(f"c_{n}", shape, dt))

        def sem(n):
            return ctx.enter_context(nc.semaphore(f"c_{n}"))

        xt = [sb(f"xt{i}", [P, NT, D]) for i in range(2)]
        yg = [sb(f"yg{i}", [P, 2, NT, D]) for i in range(2)]
        row = [sb(f"row{i}", [P, 2, NT], I32) for i in range(2)]
        carrier = sem("carrier")
        x_loaded = [sem(f"x_loaded{i}") for i in range(2)]
        gathered = [sem(f"gathered{i}") for i in range(2)]
        stored = [sem(f"stored{i}") for i in range(2)]
        row_done = sem("row_done")
        first_added = sem("first_added")
        x_done = sem("x_done")

        with nc.Block() as block:
            @block.sync
            def _(sp):
                def step(s, m):
                    fresh(sp)
                    if m:
                        sp.wait_ge(stored[m.slot], (m + -2).slot_count(16))
                        sp.sem_inc(carrier, 1)
                        sp.dma_start(xt[m.slot][:, :, :], x_in[m.index()].rearrange("(t p) d -> p t d", p=P))\
                            .then_inc(x_loaded[m.slot], 16)
                    if s:
                        sp.wait_ge(x_done, s.count(1, 1))
                        sp.sem_inc(carrier, 1)
                        sp.dma_start(x_out[s.index()].rearrange("(t p) d -> p t d", p=P), xt[s.slot][:, :, :])\
                            .then_inc(stored[s.slot], 16)

                turns_of_two(sp.Fori, step, B)
                for i in range(2):
                    sp.wait_ge(stored[i], 16 * B // 2)

            @block.gpsimd
            def _(pool):
                def step(s, m):
                    fresh(pool)
                    if m:
                        pool.wait_ge(row_done, m.count(1, 1))
                        pool.wait_ge(x_done, (m + -1).count(1))
                        pool.sem_inc(carrier, 1)
                        for k in range(2):
                            for t in range(NT):
                                pool.indirect_dma_start(
                                    yg[m.slot][:, k, t, :], None, ys,
                                    bass.IndirectOffsetOnAxis(ap=row[m.slot][:, k, t:t + 1], axis=0))\
                                    .then_inc(gathered[m.slot], 16)

                turns_of_two(pool.Fori, step, B)

            @block.vector
            def _(dve):
                def step(s, m):
                    fresh(dve)
                    if m:
                        nc.vector.tensor_copy(row[m.slot][:, :, :], yrow[:, :, bass.ds(m.index() * NT, NT)])\
                            .then_inc(row_done, 1)
                    if s:
                        dve.wait_ge(x_loaded[s.slot], s.slot_count(16))
                        dve.wait_ge(gathered[s.slot], s.slot_count(16 * 2 * NT))
                        x = xt[s.slot]
                        for k, done in enumerate((first_added, x_done)):
                            for t in range(NT):
                                last = nc.vector.scalar_tensor_tensor(
                                    x[:, t, :], yg[s.slot][:, k, t, :], gate[:, k, bass.ds(s.index() * NT + t, 1)],
                                    x[:, t, :], ALU.mult, ALU.add)
                            last.then_inc(done, 1)
                            if k == 0:
                                dve.wait_ge(first_added, s.count(1, 1))
                                dve.sem_inc(carrier, 1)

                turns_of_two(dve.Fori, step, B)


def ternary(nc, x_in, x_out, w_d, ident_d):
    ctx = ExitStack()
    with ctx:
        def sb(n, shape, dt=F32):
            return ctx.enter_context(nc.sbuf_tensor(f"t_{n}", shape, dt))

        def sem(n):
            return ctx.enter_context(nc.semaphore(f"t_{n}"))

        bank = [ctx.enter_context(nc.psum_tensor(f"t_bank{i}", [P, 512], F32)) for i in range(8)]
        ident = sb("ident", [P, P])
        ones = sb("ones", [P, P])
        w = sb("w", [P, KC, D])
        q = sb("q", [P, KC, D])
        q2 = sb("q2", [P, KC, D])
        tern = sb("tern", [P, KC, D], F32R)
        rowsum = sb("rowsum", [P, 1])
        scale = sb("scale", [P, 1])
        inverse = sb("inverse", [P, 1])
        power = sb("power", [P, NT])
        xt = [sb(f"xt{i}", [P, NT, D]) for i in range(2)]
        yt = [sb(f"yt{i}", [P, NT, D]) for i in range(2)]
        xn = [sb(f"xn{i}", [P, NT, D]) for i in range(2)]
        stats = sb("stats", [P, NT, 6])
        mv = sb("mv", [P, NT, 2])
        ve = sb("ve", [P, NT])
        rstd = sb("rstd", [P, NT])
        xh = sb("xh", [P, KC, T], F32R)
        xl = sb("xl", [P, KC, T], F32R)

        carrier = sem("carrier")
        const_loaded, setup, absum, total = (sem(n) for n in ("const_loaded", "setup", "absum", "total"))
        x_loaded = [sem(f"x_loaded{i}") for i in range(2)]
        y_stored = [sem(f"y_stored{i}") for i in range(2)]
        stats_done, var_done, ve_done, rstd_done, xn_done = (
            sem(n) for n in ("stats_done", "var_done", "ve_done", "rstd_done", "xn_done"))
        transposed = sem("transposed")
        xh_done = sem("xh_done")
        xl_done = sem("xl_done")
        projected = sem("projected")
        y_done = sem("y_done")

        with nc.Block() as block:
            @block.sync
            def _(sp):
                sp.dma_start(ident[:, :], ident_d).then_inc(const_loaded, 16)
                sp.dma_start(w[:, :, :], w_d.rearrange("(c p) n -> p c n", p=P)).then_inc(const_loaded, 16)
                sp.wait_ge(const_loaded, 32)

            @block.tensor
            def _(pe):
                pe.wait_ge(absum, 2)
                nc.tensor.matmul(bank[0][:, 0:1], ones[:, :], rowsum[:, :], start=True, stop=True).then_inc(total, 1)

            @block.vector
            def _(dve):
                nc.vector.memset(ones[:, :], 1.0)
                nc.vector.memset(power[:, :], -0.5).then_inc(absum, 1)
                dve.wait_ge(const_loaded, 32)
                nc.vector.tensor_reduce(rowsum[:, :], w[:, :, :], AX.XY, ALU.add, apply_absolute_value=True)\
                    .then_inc(absum, 1)
                dve.wait_ge(total, 1)
                nc.vector.tensor_scalar(scale[:, :], bank[0][:, 0:1], 1.0 / (D * D), EPS, ALU.mult, ALU.max)\
                    .then_inc(setup, 1)
                dve.wait_ge(setup, 1)
                nc.vector.reciprocal(inverse[:, :], scale[:, :]).then_inc(setup, 1)
                dve.wait_ge(setup, 2)
                nc.vector.tensor_scalar(q[:, :, :], w[:, :, :], inverse[:, :], None, ALU.mult).then_inc(setup, 1)
                dve.wait_ge(setup, 3)
                magic = 1.5 * 2.0 ** 23
                nc.vector.tensor_scalar(q2[:, :, :], q[:, :, :], magic, None, ALU.add).then_inc(setup, 1)
                dve.wait_ge(setup, 4)
                nc.vector.tensor_scalar(q[:, :, :], q2[:, :, :], magic, -1.0, ALU.subtract, ALU.max).then_inc(setup, 1)
                dve.wait_ge(setup, 5)
                nc.vector.tensor_scalar(tern[:, :, :], q[:, :, :], 1.0, None, ALU.min).then_inc(setup, 1)
                dve.wait_ge(setup, 6)

        with nc.Block() as block:
            @block.sync
            def _(sp):
                def step(s, m):
                    fresh(sp)
                    if m:
                        sp.wait_ge(y_done, (m + -1).count(1))
                        sp.sem_inc(carrier, 1)
                        sp.dma_start(xt[m.slot][:, :, :], x_in[m.index()].rearrange("(t p) d -> p t d", p=P))\
                            .then_inc(x_loaded[m.slot], 16)
                    if s:
                        sp.wait_ge(y_done, s.count(1, 1))
                        sp.sem_inc(carrier, 1)
                        sp.dma_start(x_out[s.index()].rearrange("(t p) d -> p t d", p=P), yt[s.slot][:, :, :])\
                            .then_inc(y_stored[s.slot], 16)

                turns_of_two(sp.Fori, step, B)
                for i in range(2):
                    sp.wait_ge(y_stored[i], 16 * B // 2)

            @block.gpsimd
            def _(pool):
                def step(s, m):
                    fresh(pool)
                    if m:
                        pool.wait_ge(var_done, m.count(1, 1))
                        pool.sem_inc(carrier, 1)
                        nc.gpsimd.tensor_scalar_add(ve[:, :], mv[:, :, 1], EPS).then_inc(ve_done, 1)
                        pool.wait_ge(ve_done, m.count(1, 1))
                        nc.gpsimd.tensor_tensor(rstd[:, :], ve[:, :], power[:, :], ALU.pow).then_inc(rstd_done, 1)

                turns_of_two(pool.Fori, step, B)

            @block.scalar
            def _(act):
                def step(s, m):
                    fresh(act)
                    if m:
                        for c in range(KC):
                            act.wait_ge(transposed, m.count(KC, c + 1))
                            if c == 0:
                                act.wait_ge(projected, m.count(2))
                            nc.scalar.copy(xh[:, c, :], bank[c][:, :]).then_inc(xh_done, 1)

                turns_of_two(act.Fori, step, B)

            @block.vector
            def _(dve):
                def step(s, m):
                    fresh(dve)
                    if m:
                        dve.wait_ge(x_loaded[m.slot], m.slot_count(16))
                        x = xt[m.slot]
                        for t in range(NT):
                            last = nc.vector.bn_stats(stats[:, t, :], x[:, t, :])
                        last.then_inc(stats_done, 1)
                        dve.wait_ge(stats_done, m.count(1, 1))
                        dve.sem_inc(carrier, 1)
                        for t in range(NT):
                            last = nc.vector.bn_aggr(mv[:, t, :], stats[:, t, :])
                        last.then_inc(var_done, 1)
                    if s:
                        dve.wait_ge(y_stored[s.slot], (s + -2).slot_count(16))
                        for n in range(2):
                            dve.wait_ge(projected, s.count(2, n + 1))
                            last = nc.vector.scalar_tensor_tensor(
                                yt[s.slot][:, 2 * n:2 * n + 2, :],
                                bank[4 + 2 * s.slot + n][:, :].rearrange("p (t d) -> p t d", t=2),
                                scale[:, :], xt[s.slot][:, 2 * n:2 * n + 2, :], ALU.mult, ALU.add)
                        last.then_inc(y_done, 1)
                    if m:
                        dve.wait_ge(rstd_done, m.count(1, 1))
                        dve.wait_ge(transposed, (m + -1).count(KC))
                        for t in range(NT):
                            last = nc.vector.tensor_scalar(xn[m.slot][:, t, :], x[:, t, :], mv[:, t, 0:1],
                                                           rstd[:, t:t + 1], ALU.subtract, ALU.mult)
                        last.then_inc(xn_done, 1)
                        for c in range(KC):
                            dve.wait_ge(xh_done, m.count(KC, c + 1))
                            nc.vector.tensor_tensor(xl[:, c, :], bank[c][:, :], xh[:, c, :].bitcast(F32), ALU.subtract)\
                                .then_inc(xl_done, 1)

                turns_of_two(dve.Fori, step, B)

            @block.tensor
            def _(pe):
                def step(s, m):
                    fresh(pe)
                    if s:
                        pe.wait_ge(xl_done, (s + 1).count(KC))
                        for n in range(2):
                            for t in range(2 * n, 2 * n + 2):
                                p = 0
                                for c in range(KC):
                                    for x in (xh, xl):
                                        last = nc.tensor.matmul(bank[4 + 2 * s.slot + n][:, (t % 2) * D:(t % 2 + 1) * D],
                                                                x[:, c, t * P:(t + 1) * P], tern[:, c, :],
                                                                start=(p == 0), stop=(p == 2 * KC - 1))
                                        p += 1
                            last.then_inc(projected, 1)
                    if m:
                        pe.wait_ge(xn_done, m.count(1, 1))
                        pe.wait_ge(xl_done, m.count(KC))
                        for c in range(KC):
                            for t in range(NT):
                                last = nc.tensor.transpose(bank[c][:, t * P:(t + 1) * P],
                                                           xn[m.slot][:, t, c * P:(c + 1) * P], ident[:, :])
                            last.then_inc(transposed, 1)

                turns_of_two(pe.Fori, step, B)



def rotary_tables():
    theta = (1.0 / 10000.0 ** (np.arange(DH // 2, dtype=np.float32) / np.float32(DH // 2))).astype(np.float32)
    f = np.arange(T, dtype=np.float32)[:, None] * theta[None, :]
    return np.stack([np.repeat(g(f).T, H, axis=0) for g in (np.cos, np.sin)]).astype(np.float32)


def xpos_tables():
    inv = (1.0 / 10000.0 ** (np.arange(0, DH, 2, dtype=np.float32) / np.float32(DH))).astype(np.float32)
    t = np.arange(T, dtype=np.float32)
    f = t[:, None] * inv[None, :]
    base = ((np.arange(0, DH, 2, dtype=np.float32) + np.float32(0.4 * DH)) / np.float32(1.4 * DH)).astype(np.float32)
    power = ((t - T // 2) / np.float32(512.0)).astype(np.float32)
    half = (base[None, :] ** power[:, None]).astype(np.float32)
    full = np.concatenate([half, half], axis=-1)
    out = []
    for s in (full, (np.float32(1.0) / full).astype(np.float32)):
        for odd in range(2):
            for g in (np.cos, np.sin):
                out.append(np.repeat((g(f) * s[:, odd::2]).T, H, axis=0))
    return np.stack(out).astype(np.float32)


def masks():
    r, c = np.arange(P)[:, None], np.arange(P)[None, :]
    lower = np.where(c <= r, 0.0, MASKED)
    before = np.where(c > r, 0.0, MASKED)
    return np.stack([np.tile(m, (1, 512 // m.shape[1])) for m in (
        np.concatenate([before, lower], 1), lower,
        np.concatenate([lower.T, before.T], 1), lower.T)], 1).astype(mybir.dt.np(BF16))


def chunked(w):
    return np.ascontiguousarray(w.reshape(KC, P, -1).transpose(1, 0, 2))


def kernel(**inputs):
    import concourse.bacc as bacc
    from concourse.bass_utils import run_bass_kernel_spmd

    a = {k: np.asarray(v) for k, v in inputs.items()}
    half = DH // 2
    by_halves = np.array([[h * DH + b * half + d for d in range(half) for h in range(H)] for b in range(2)]).reshape(-1)
    by_parity = np.array([[h * DH + 2 * d + b for d in range(half) for h in range(H)] for b in range(2)]).reshape(-1)

    def padded_out(w):
        out = np.zeros((NG, HG, 32, D), np.float32)
        out[:, :, :DH] = w.reshape(NG, HG, DH, D)
        return np.ascontiguousarray(out.reshape(NG, P, D).transpose(1, 0, 2))

    wqkv = a["L0_attn_Wqkv"]
    w0 = np.concatenate([wqkv[:, :D][:, by_halves], wqkv[:, D:2 * D][:, by_halves], wqkv[:, 2 * D:]], 1)
    w1 = np.concatenate([a["L1_attn_Wq"].T[:, by_parity], a["L1_attn_Wv"].T[:, by_parity], a["L1_attn_Wk"].T], 1)
    bqk = np.stack([a["L1_attn_bq"][by_parity][:P], a["L1_attn_bq"][by_parity][P:],
                    a["L1_attn_bv"][by_parity][:P], a["L1_attn_bv"][by_parity][P:]], 1)
    arrays = {
        "x": a["L0_attn_x"],
        "w0": chunked(w0), "wo0": padded_out(a["L0_attn_Wout"]), "tab0": rotary_tables(),
        "w1": chunked(w1), "wo1": padded_out(a["L1_attn_Wo"].T), "tab1": xpos_tables(),
        "bqk": bqk, "bv": a["L1_attn_bk"], "bo": a["L1_attn_bo"],
        "ident": np.eye(P, dtype=np.float32), "identb": np.eye(P).astype(mybir.dt.np(BF16)), "masks": masks(),
        "wr": chunked(a["L0_ffn_Wr"].T), "br": a["L0_ffn_br"], "bn": a["L0_ffn_biases_N"],
        "we1": np.stack([chunked(w) for w in a["L0_ffn_Wl1"]]),
        "be1": np.ascontiguousarray(a["L0_ffn_bl1"].reshape(NE, 2 * FC, P).transpose(0, 2, 1)),
        "we2": np.ascontiguousarray(a["L0_ffn_Wl2"].reshape(NE, FC, P, D).transpose(0, 2, 1, 3)),
        "be2": a["L0_ffn_bl2"],
        "below": np.tril(np.ones((NE, NE), np.float32), -1),
        "before": np.triu(np.ones((P, P)), 1).astype(mybir.dt.np(BF16)),
        "starts": np.concatenate([np.arange(NE), np.tril(np.ones((NE, NE)), -1).reshape(-1), np.arange(TILES),
                                  TILE * np.arange(B * T // TILE)]).astype(np.float32),
        "wt": np.ascontiguousarray(a["L1_ffn_weight"].T),
    }
    arrays = {k: np.ascontiguousarray(v) for k, v in arrays.items()}
    nc = bacc.Bacc("TRN2", target_bir_lowering=False, num_devices=1)
    d = {k: nc.dram_tensor(f"in_{k}", v.shape, mybir.dt.from_np(v.dtype), kind="ExternalInput").ap()
         for k, v in arrays.items()}
    out = nc.dram_tensor("out", [B, T, D], F32, kind="ExternalOutput").ap()
    x1, x2, x3 = (nc.dram_tensor(n, [B, T, D], F32, kind="Internal").ap() for n in ("x1", "x2", "x3"))

    consts = (d["ident"], d["identb"], d["masks"])
    attention(nc, "a0", d["x"], x1, d["w0"], d["wo0"], d["tab0"], None, True, DH ** -0.5, consts)
    xs = nc.dram_tensor("xs", [NE * REGION, D], F32, kind="Internal").ap()
    ys = nc.dram_tensor("ys", [TILES * TILE, D], F32, kind="Internal").ap()
    with ExitStack() as ctx:
        gate, place, expert = (ctx.enter_context(nc.sbuf_tensor(n, [P, 2, B * NT], F32))
                               for n in ("gate", "place", "expert"))
        taken = ctx.enter_context(nc.sbuf_tensor("taken", [P, NE], F32))
        yrow = ctx.enter_context(nc.sbuf_tensor("yrow", [P, 2, B * NT], I32))
        choice = (gate, place, expert, taken)
        route(nc, x1, xs, d["wr"], d["br"], d["bn"], d["below"], d["before"], d["ident"], choice)
        experts(nc, xs, ys, d["we1"], d["be1"], d["we2"], d["be2"], d["starts"], d["ident"], choice, yrow)
        combine(nc, x1, x2, ys, gate, yrow)
    attention(nc, "a1", x2, x3, d["w1"], d["wo1"], d["tab1"], (d["bqk"], d["bv"], d["bo"]), False,
              (DH * H) ** -0.5, consts)
    ternary(nc, x3, out, d["wt"], d["ident"])
    r = run_bass_kernel_spmd(nc, [{f"in_{k}": v for k, v in arrays.items()}], core_ids=[0])
    return r.results[0]["out"]
```
